# Optimizing a Trainium2 kernel written in Bass

```python
import numpy as np
import jax
import jax.numpy as jnp

def _softmax(x, axis=-1):
    return jax.nn.softmax(x, axis=axis)
def _gelu(x):
    return jax.nn.gelu(x, approximate=True)
def _silu(x):
    return jax.nn.silu(x)
def _sigmoid(x):
    return jax.nn.sigmoid(x)
def _layernorm(x, axis=-1, eps=1e-5):
    m = jnp.mean(x, axis=axis, keepdims=True)
    v = jnp.var(x, axis=axis, keepdims=True)
    return (x - m) / jnp.sqrt(v + eps)
def _scatter_add(tgt, idx, src, axis=0):
    return tgt.at[idx].add(src)
def _segment_sum(src, seg, n):
    return jax.ops.segment_sum(src, seg, n)

kernel_name = 'mk_conv_preact_d2_conv_nchw32_6c2059'

def setup_inputs(seed: int = 0):
    np.random.seed(seed)
    _w = jnp.asarray
    def _rec_inputs():
        import jax
        import jax.numpy as jnp
        _gk = jax.random.key(seed)
        x = -0.0002928 + 1 * jax.random.normal(jax.random.fold_in(_gk, 1), (8, 32, 128, 128), jnp.float32)
        return x
    x = _rec_inputs()
    def _L0_conv_setup():
        import jax, jax.numpy as jnp
        import numpy as np
        key = jax.random.key(seed)
        k1, k2, k3 = jax.random.split(key, 3)
        x = jax.random.normal(k1, (8, 32, 128, 128), dtype=jnp.float32)
        weight = jax.random.normal(k2, (32, 32, 3, 3), dtype=jnp.float32)
        bias = jax.random.normal(k3, (32,), dtype=jnp.float32)
        return {'x': x, 'weight': weight, 'bias': bias, 'stride': 1, 'padding': 1}
    _L0_conv_all = _L0_conv_setup()
    _L0_conv_in = {k: v for k, v in _L0_conv_all.items() if k in ('weight', 'bias', )}
    del _L0_conv_all

    def _L1_conv_setup():
        import jax, jax.numpy as jnp
        import numpy as np
        B, C_IN, H, W = (16, 32, 256, 256)
        C_OUT, KH, KW = (32, 3, 3)
        STRIDE = (1, 1)
        PADDING = (1, 1)
        key = jax.random.key(seed)
        kx, kw = jax.random.split(key)
        x = jax.random.normal(kx, (B, C_IN, H, W), dtype=jnp.float32)
        fan_in = C_IN * KH * KW
        bound = float(np.sqrt(6.0 / fan_in))
        weight = jax.random.uniform(kw, (C_OUT, C_IN, KH, KW), dtype=jnp.float32, minval=-bound, maxval=bound)
        bias = jnp.zeros((C_OUT,), dtype=jnp.float32)
        return {'x': x, 'weight': weight, 'bias': bias}
    _L1_conv_all = _L1_conv_setup()
    _L1_conv_in = {k: v for k, v in _L1_conv_all.items() if k in ('weight', 'bias', )}
    del _L1_conv_all

    return {
        "x": x,
        "L0_conv_weight": _L0_conv_in["weight"],
        "L0_conv_bias": _L0_conv_in["bias"],
        "L1_conv_weight": _L1_conv_in["weight"],
        "L1_conv_bias": _L1_conv_in["bias"],
    }

def reference(x, L0_conv_weight, L0_conv_bias, L1_conv_weight, L1_conv_bias):
    import jax
    import jax.numpy as jnp
    def _L0_conv_ref(x, weight, bias, stride, padding):
        import jax, jax.numpy as jnp
        import numpy as np
        B, C, H, W = x.shape
        O, _, K, _ = weight.shape
        fft_H = 2 ** int(np.ceil(np.log2(H + K - 1)))
        fft_W = 2 ** int(np.ceil(np.log2(W + K - 1)))
        px = jnp.pad(x, ((0, 0), (0, 0), (0, fft_H - H), (0, fft_W - W)))
        fx = jnp.fft.fft2(px, norm='ortho')
        pw = jnp.pad(weight, ((0, 0), (0, 0), (0, fft_H - K), (0, fft_W - K)))
        wf = jnp.fft.fft2(pw, norm='ortho')
        fout = jnp.einsum('bihw,oihw->bohw', fx, wf)
        sp = jnp.fft.ifft2(fout, norm='ortho').real
        out_h = (H + 2 * padding - K) // stride + 1
        out_w = (W + 2 * padding - K) // stride + 1
        sh = (fft_H - out_h) // 2
        sw = (fft_W - out_w) // 2
        out = sp[:, :, sh:sh + out_h, sw:sw + out_w]
        return out + bias[None, :, None, None]

    def _L1_conv_ref(x, weight, bias):
        import jax, jax.numpy as jnp
        import numpy as np
        B, C_IN, H, W = (16, 32, 256, 256)
        C_OUT, KH, KW = (32, 3, 3)
        STRIDE = (1, 1)
        PADDING = (1, 1)
        out = jax.lax.conv_general_dilated(x, weight, window_strides=STRIDE, padding=[(PADDING[0], PADDING[0]), (PADDING[1], PADDING[1])], dimension_numbers=('NCHW', 'OIHW', 'NCHW'))
        return out + bias[None, :, None, None]

    def _gn(v, G=16, eps=1e-5):
        B_, C_, H_, W_ = v.shape
        g = v.reshape(B_, G, C_ // G, H_, W_)
        m = jnp.mean(g, axis=(2, 3, 4), keepdims=True)
        s = jnp.var(g, axis=(2, 3, 4), keepdims=True)
        return ((g - m) / jnp.sqrt(s + eps)).reshape(v.shape)

    def _ln_c(v, eps=1e-6):
        m = jnp.mean(v, axis=1, keepdims=True)
        s = jnp.var(v, axis=1, keepdims=True)
        return (v - m) / jnp.sqrt(s + eps)

    def _ln_t(v, eps=1e-5):
        m = jnp.mean(v, axis=-1, keepdims=True)
        s = jnp.var(v, axis=-1, keepdims=True)
        return (v - m) / jnp.sqrt(s + eps)

    def _to_tokens(v):
        B_, C_, H_, W_ = v.shape
        return v.reshape(B_, C_, H_ * W_).transpose(0, 2, 1)
    def _from_tokens(t, like):
        B_, C_, H_, W_ = like.shape
        return t.transpose(0, 2, 1).reshape(B_, C_, H_, W_)

    x = x + _L0_conv_ref(_gn(x), L0_conv_weight, L0_conv_bias, 1, 1)
    x = x + _L1_conv_ref(_gn(x), L1_conv_weight, L1_conv_bias)
    return x


_drawn_inputs = setup_inputs


def setup_inputs(seed=0):
    import zlib

    import numpy as np

    out = dict(_drawn_inputs(seed))
    spreads = {'L1_conv_bias': (0.0, 0.1)}
    factors = {}
    for name, (base, spread) in spreads.items():
        noise = np.random.default_rng([zlib.crc32(name.encode()), seed]).standard_normal(out[name].shape)
        drawn = base * np.exp(spread * noise) if base else spread * noise
        out[name] = jnp.asarray(drawn.astype(out[name].dtype))
    for name, factor in factors.items():
        out[name] = (out[name] * factor).astype(out[name].dtype)
    return out
```

```python
from contextlib import ExitStack

import concourse.bass as bass
from concourse import mybir

F32 = mybir.dt.float32
F32R = mybir.dt.float32r
ALU = mybir.AluOpType
ACT = mybir.ActivationFunctionType

P = 128
SIDE = 65
CELLS = SIDE * SIDE
OUT = 64
VALID = OUT * OUT
REG = 34
SRC = SIDE - REG
EPS = 1e-5
FFT_SCALE = 1.0 / 256.0
PAD_K = CELLS / VALID

L0_ROWS = [(0, 12), (12, 11), (23, 11)]
L1_ROWS = 8
CH1 = OUT // L1_ROWS
HD_ROWS = [(0, 9)] + [(9 + 8 * k, 8) for k in range(7)]
REST = [(r0, n, REG, SIDE - REG) for r0, n in L0_ROWS] + [(34, 7, 0, SIDE)] + [
    (41 + 6 * k, 6, 0, SIDE) for k in range(4)]
N0, NR = len(L0_ROWS), len(REST)
PARTS = [(s, hl) for s in range(4) for hl in ("hh", "hl", "lh")]


def conv_blocks(nc, x, w0, w1, ident, g0, g1, bias0, bias1, out):
    images = x.shape[0]
    with ExitStack() as ctx:
        def sb(name, shape, dt=F32):
            return ctx.enter_context(nc.sbuf_tensor(name, shape, dt))

        def ps(name, shape):
            return ctx.enter_context(nc.psum_tensor(name, shape, F32))

        def sem(name):
            return ctx.enter_context(nc.semaphore(name))

        xs = [sb(f"x_{p}", [P, SIDE, SIDE]) for p in range(2)]
        hi1 = [sb(f"hi1_{p}", [P, SIDE, SIDE], F32R) for p in range(2)]
        lo1 = [sb(f"lo1_{p}", [P, SIDE, SIDE], F32R) for p in range(2)]
        hl0 = sb("hl0", [P, 2, REG + 1, REG + 1], F32R)
        w0_base, w1_base = sb("w0_base", [P, 512]), sb("w1_base", [P, 512])
        identity = sb("identity", [P, 512])
        w_scaled = sb("w_scaled", [P, 512])
        w0_hi, w0_lo = sb("w0_hi", [P, 512], F32R), sb("w0_lo", [P, 512], F32R)
        w1_hi = [sb(f"w1_hi_{p}", [P, 512], F32R) for p in range(2)]
        w1_lo = [sb(f"w1_lo_{p}", [P, 512], F32R) for p in range(2)]
        group0, group1 = sb("group0", [P, P]), sb("group1", [P, P])
        b0, b1 = sb("b0", [P, 1]), sb("b1", [P, 1])
        b0_2, b0_sq = sb("b0_2", [P, 1]), sb("b0_sq", [P, 1])
        bn = [sb(f"bn_{p}", [P, N0 + NR, 6]) for p in range(2)]
        mv = sb("mv", [P, 2])
        mom = sb("mom", [P, 2])
        tmp = sb("tmp", [P, 8])
        neg_mean0 = sb("neg_mean0", [P, 1])
        neg_mean1 = [sb(f"neg_mean1_{p}", [P, 1]) for p in range(2)]
        out_bias = [sb(f"out_bias_{p}", [P, 1]) for p in range(2)]
        var, std, rstd = sb("var", [P, 2]), sb("std", [P, 2]), sb("rstd", [P, 2])
        stage = sb("stage", [P, CH1 // 2, 2 * 512])

        ps1 = ps("ps1", [P, 4, 512])
        ps0 = ps("ps0", [P, N0, 512])
        psg = ps("psg", [P, 4])

        consts_in = sem("consts_in")
        x_in = [sem(f"x_in_{p}") for p in range(2)]
        zeroed = sem("zeroed")
        dve_done = sem("dve_done")
        moments0, moments1 = sem("moments0"), sem("moments1")
        sums0, sums1 = sem("sums0"), sem("sums1")
        var0_ready, var1_ready = sem("var0_ready"), sem("var1_ready")
        std0_ready, std1_ready = sem("std0_ready"), sem("std1_ready")
        mean0, mean1 = sem("mean0"), sem("mean1")
        hi0_ready, hl0_ready = sem("hi0_ready"), sem("hl0_ready")
        w0_ready, w1_ready = sem("w0_ready"), sem("w1_ready")
        conv0 = sem("conv0")
        hd1_ready, lo1_ready = sem("hd1_ready"), sem("lo1_ready")
        conv1, evicted = sem("conv1"), sem("evicted")
        stored = [sem(f"stored_{k}") for k in range(CH1 // 2)]
        block = ctx.enter_context(nc.Block())

        loops = (images - 2) // 2

        @block.sync
        def _(sp):
            def load(j, par):
                sp.dma_start(xs[par][:].rearrange("p y x -> p (y x)"), x[2 * j + par]).then_inc(x_in[par], 16)

            def store(j, par):
                for k in range(CH1 // 2):
                    sp.wait_ge(evicted, CH1 * (2 * j + par) + 2 * k + 2)
                    sp.dma_start(out[2 * j + par, :, k * 1024:(k + 1) * 1024], stage[:, k, :]).then_inc(stored[k], 16)

            load(0, 0)
            for dst, src in ((b0, bias0), (b1, bias1), (group0, g0), (w0_base, w0), (group1, g1), (w1_base, w1),
                             (identity, ident)):
                sp.dma_start(dst[:], src).then_inc(consts_in, 16)
            load(0, 1)

            def step(j, par, ahead):
                if ahead:
                    sp.wait_ge(lo1_ready, CH1 * (2 * j + par + 1))
                    load(j + 1, par)
                store(j, par)

            with sp.Fori(0, loops) as j:
                step(j, 0, True)
                step(j, 1, True)
            step(loops, 0, False)
            step(loops, 1, False)
            for k in range(CH1 // 2):
                sp.wait_ge(stored[k], 16 * images)

        @block.vector
        def _(dve):
            SETUP, A_STEPS, B_STEPS = 2, 11, 19
            count = {"base": 0, "n": 0, "limit": 0}

            def begin(base, limit):
                count.update(base=base, n=0, limit=limit)

            def done(ins):
                count["n"] += 1
                ins.then_inc(dve_done, 1)

            def settle():
                dve.wait_ge(dve_done, count["base"] + count["n"])

            def end():
                assert count["n"] == count["limit"], count

            def variance(sums, col, ready):
                done(nc.vector.tensor_copy(tmp[:, 0:2], sums))
                settle()
                done(nc.vector.scalar_tensor_tensor(tmp[:, 2:3], tmp[:, 0:1], tmp[:, 0:1], tmp[:, 1:2], ALU.mult, ALU.subtract))
                settle()
                nc.vector.tensor_scalar(var[:, col:col + 1], tmp[:, 2:3], -1.0, EPS, ALU.mult,
                                        ALU.add).then_inc(ready, 1)

            def inv_std(col):
                v, r = var[:, col:col + 1], tmp[:, 4:5]
                done(nc.vector.reciprocal(r, std[:, col:col + 1]))
                settle()
                done(nc.vector.scalar_tensor_tensor(tmp[:, 5:6], r, r, v, ALU.mult, ALU.mult))
                settle()
                done(nc.vector.tensor_scalar(tmp[:, 6:7], tmp[:, 5:6], -0.5, 1.5, ALU.mult, ALU.add))
                settle()
                done(nc.vector.tensor_scalar(rstd[:, col:col + 1], r, tmp[:, 6:7], None, ALU.mult))

            def aggregate(par):
                settle()
                nc.vector.memset(tmp[:, 7:8], 0.0)
                done(nc.vector.bn_aggr(mv[:], bn[par][:].rearrange("p k s -> p (k s)")))

            def prepare0(j, par, base):
                begin(base, A_STEPS)
                n = 2 * j + par
                X = xs[par]
                dve.wait_ge(x_in[par], 16 * (j + 1))
                for k, (r0, rows) in enumerate(L0_ROWS):
                    nc.vector.bn_stats(bn[par][:, k, :], X[:, r0:r0 + rows, 0:REG])
                for k, (r0, rows, c0, cols) in enumerate(REST):
                    last = nc.vector.bn_stats(bn[par][:, N0 + k, :], X[:, r0:r0 + rows, c0:c0 + cols])
                done(last)
                aggregate(par)
                settle()
                nc.vector.tensor_copy(mom[:, 0:1], mv[:, 0:1])
                nc.vector.scalar_tensor_tensor(mom[:, 1:2], mv[:, 0:1], mv[:, 0:1], mv[:, 1:2], ALU.mult,
                                               ALU.add).then_inc(moments0, 1)
                dve.wait_ge(sums0, n + 1)
                nc.vector.tensor_scalar(neg_mean0[:], psg[:, 0:1], -1.0, None, ALU.mult).then_inc(mean0, 1)
                variance(psg[:, 0:2], 0, var0_ready)
                dve.wait_ge(std0_ready, n + 1)
                inv_std(0)
                settle()
                done(nc.vector.tensor_scalar(tmp[:, 7:8], rstd[:, 0:1], FFT_SCALE, None, ALU.mult))
                settle()
                done(nc.vector.tensor_scalar(w0_hi[:], w0_base[:], tmp[:, 7:8], None, ALU.mult))
                settle()
                nc.vector.scalar_tensor_tensor(w0_lo[:], w0_base[:], tmp[:, 7:8], w0_hi[:].bitcast(F32), ALU.mult,
                                               ALU.subtract).then_inc(w0_ready, 1)
                dve.wait_ge(hi0_ready, n + 1)
                done(nc.vector.scalar_tensor_tensor(hl0[:, 1, 0:REG, 0:REG], X[:, SRC:SIDE, SRC:SIDE], neg_mean0[:, 0:1],
                                                    hl0[:, 0, 0:REG, 0:REG].bitcast(F32), ALU.add, ALU.subtract))
                settle()
                z = hl0[:].bitcast(F32)
                nc.vector.memset(z[64:128, :, REG - 1:REG, 0:REG], 0.0)
                nc.vector.memset(z[32:64, :, 0:REG, REG - 1:REG], 0.0)
                nc.vector.memset(z[96:128, :, 0:REG - 1, REG - 1:REG], 0.0).then_inc(hl0_ready, 1)
                end()

            def prepare1(j, par, base):
                begin(base, B_STEPS)
                n = 2 * j + par
                X = xs[par]
                for k, (r0, rows) in enumerate(L0_ROWS):
                    dve.wait_ge(conv0, N0 * n + k + 1)
                    area = X[:, r0:r0 + rows, 0:REG]
                    done(nc.vector.tensor_tensor(area, area, ps0[:, k, 0:rows * REG].rearrange("p (y x) -> p y x", x=REG),
                                                 ALU.add))
                settle()
                nc.vector.memset(X[0:64, 0:1, 0:REG], 0.0)
                nc.vector.memset(X[0:32, 1:REG, 0:1], 0.0)
                done(nc.vector.memset(X[64:96, 0:REG, 0:1], 0.0))
                settle()
                for k, (r0, rows) in enumerate(L0_ROWS):
                    last = nc.vector.bn_stats(bn[par][:, k, :], X[:, r0:r0 + rows, 0:REG])
                done(last)
                aggregate(par)
                settle()
                done(nc.vector.tensor_scalar(mom[:, 0:1], mv[:, 0:1], PAD_K, b0[:, 0:1], ALU.mult, ALU.add))
                done(nc.vector.scalar_tensor_tensor(tmp[:, 0:1], mv[:, 0:1], mv[:, 0:1], mv[:, 1:2], ALU.mult, ALU.add))
                settle()
                done(nc.vector.tensor_scalar(tmp[:, 1:2], mom[:, 0:1], b0_2[:, 0:1], b0_sq[:, 0:1], ALU.mult,
                                             ALU.subtract))
                settle()
                nc.vector.scalar_tensor_tensor(mom[:, 1:2], tmp[:, 0:1], PAD_K, tmp[:, 1:2], ALU.mult,
                                               ALU.add).then_inc(moments1, 1)
                dve.wait_ge(sums1, n + 1)
                wait_before(evicted, CH1, j, par)
                done(nc.vector.tensor_tensor(neg_mean1[par][:], b0[:], psg[:, 2:3], ALU.subtract))
                done(nc.vector.tensor_tensor(out_bias[par][:], b1[:], psg[:, 2:3], ALU.add))
                variance(psg[:, 2:4], 1, var1_ready)
                pad = neg_mean1[par]
                for p0, p1, edge in ((0, 64, X[0:64, 0, :]), (64, 128, X[64:128, SIDE - 1, :]),
                                     (0, 32, X[0:32, 1:SIDE, 0]), (64, 96, X[64:96, 0:SIDE - 1, 0]),
                                     (32, 64, X[32:64, 1:SIDE, SIDE - 1]), (96, 128, X[96:128, 0:SIDE - 1, SIDE - 1])):
                    last = nc.vector.tensor_scalar(edge, pad[p0:p1, 0:1].broadcast_to([p1 - p0, edge.shape[1]]), -1.0,
                                                   None, ALU.mult)
                last.then_inc(mean1, 1)
                dve.wait_ge(std1_ready, n + 1)
                inv_std(1)
                settle()
                done(nc.vector.scalar_tensor_tensor(w_scaled[:], w1_base[:], rstd[:, 1:2], identity[:], ALU.mult, ALU.add))
                settle()
                wait_before(conv1, CH1, j, par)
                done(nc.vector.tensor_copy(w1_hi[par][:], w_scaled[:]))
                settle()
                nc.vector.tensor_tensor(w1_lo[par][:], w_scaled[:], w1_hi[par][:].bitcast(F32),
                                        ALU.subtract).then_inc(w1_ready, 1)
                end()

            def wait_before(s, per, j, par):
                if not (isinstance(j, int) and j == 0):
                    dve.wait_ge(s, per * (2 * j + par - 1))

            nc.vector.memset(hl0[:].bitcast(F32), 0.0).then_inc(zeroed, 1)
            dve.wait_ge(zeroed, 1)
            dve.wait_ge(consts_in, 7 * 16)
            done(nc.vector.tensor_scalar(b0_2[:], b0[:], 2.0, None, ALU.mult))
            done(nc.vector.tensor_tensor(b0_sq[:], b0[:], b0[:], ALU.mult))
            settle()
            per = A_STEPS + B_STEPS
            prepare0(0, 0, SETUP)
            prepare1(0, 0, SETUP + A_STEPS)
            prepare0(0, 1, SETUP + per)

            def step(j, par, one, two):
                base = SETUP + per + A_STEPS + per * (2 * j + par)
                if one:
                    prepare1(j + par, 1 - par, base)
                if two:
                    prepare0(j + 1, par, base + B_STEPS)

            step(0, 0, True, True)
            step(0, 1, True, True)
            with dve.Fori(1, loops) as j:
                step(j, 0, True, True)
                step(j, 1, True, True)
            step(loops, 0, True, False)

        @block.scalar
        def _(act):
            def high0(j, par):
                n = 2 * j + par
                act.wait_ge(var0_ready, n + 1)
                nc.scalar.activation(std[:, 0:1], var[:, 0:1], ACT.Sqrt).then_inc(std0_ready, 1)
                act.wait_ge(mean0, n + 1)
                if not (isinstance(n, int) and n == 0):
                    act.wait_ge(conv0, N0 * n)
                nc.scalar.activation(hl0[:, 0, 0:REG, 0:REG], xs[par][:, SRC:SIDE, SRC:SIDE], ACT.Identity,
                                     bias=neg_mean0[:, 0:1]).then_inc(hi0_ready, 1)

            def high1(j, par, k):
                n = 2 * j + par
                if k == 0:
                    act.wait_ge(var1_ready, n + 1)
                    nc.scalar.activation(std[:, 1:2], var[:, 1:2], ACT.Sqrt).then_inc(std1_ready, 1)
                    act.wait_ge(mean1, n + 1)
                    if not (isinstance(j, int) and j == 0):
                        act.wait_ge(conv1, CH1 * (n - 1))
                r0, rows = HD_ROWS[k]
                src = xs[par][:, r0:r0 + rows, :]
                nc.scalar.activation(hi1[par][:, r0:r0 + rows, :], src, ACT.Identity, bias=neg_mean1[par][:, 0:1])
                nc.scalar.activation(src, src, ACT.Identity, bias=neg_mean1[par][:, 0:1]).then_inc(hd1_ready, 1)

            def evict(j, par, k):
                n = 2 * j + par
                act.wait_ge(conv1, CH1 * n + k + 1)
                if k % 2 == 0 and not (isinstance(n, int) and n == 0):
                    act.wait_ge(stored[k // 2], 16 * n)
                nc.scalar.activation(stage[:, k // 2, 512 * (k % 2):512 * (k % 2) + 512], ps1[:, k % 4, :], ACT.Identity,
                                     bias=out_bias[par][:, 0:1]).then_inc(evicted, 1)

            high0(0, 0)
            for k in range(CH1):
                high1(0, 0, k)
            high0(0, 1)

            def step(j, par, one, two):
                for k in range(CH1):
                    if k == 7 and two:
                        high0(j + 1, par)
                    evict(j, par, k)
                    if one and 3 <= k < 7:
                        high1(j + par, 1 - par, 2 * (k - 3))
                        high1(j + par, 1 - par, 2 * (k - 3) + 1)

            step(0, 0, True, True)
            step(0, 1, True, True)
            with act.Fori(1, loops) as j:
                step(j, 0, True, True)
                step(j, 1, True, True)
            step(loops, 0, True, False)
            step(loops, 1, False, False)

        @block.gpsimd
        def _(pool):
            def low1(j, par):
                n = 2 * j + par
                for k, (r0, rows) in enumerate(HD_ROWS):
                    pool.wait_ge(hd1_ready, CH1 * n + k + 1)
                    if k == 0 and not (isinstance(j, int) and j == 0):
                        pool.wait_ge(conv1, CH1 * (n - 1))
                    part = slice(r0, r0 + rows)
                    nc.gpsimd.tensor_tensor(lo1[par][:, part, :], xs[par][:, part, :],
                                            hi1[par][:, part, :].bitcast(F32), ALU.subtract).then_inc(lo1_ready, 1)

            low1(0, 0)
            low1(0, 1)
            with pool.Fori(1, images // 2) as j:
                low1(j, 0)
                low1(j, 1)

        @block.tensor
        def _(pe):
            def group_sums0(n):
                pe.wait_ge(moments0, n + 1)
                nc.tensor.matmul(psg[:, 0:2], group0[:], mom[:], start=True, stop=True).then_inc(sums0, 1)

            def group_sums1(n):
                pe.wait_ge(moments1, n + 1)
                nc.tensor.matmul(psg[:, 2:4], group1[:], mom[:], start=True, stop=True).then_inc(sums1, 1)

            def block0(n):
                pe.wait_ge(hl0_ready, n + 1)
                pe.wait_ge(w0_ready, n + 1)
                for k, (r0, rows) in enumerate(L0_ROWS):
                    if k == 0 and not (isinstance(n, int) and n == 0):
                        pe.wait_ge(moments1, n)
                    acc = ps0[:, k, 0:rows * REG].rearrange("p (y x) -> p y x", x=REG)
                    for i, (s, hl) in enumerate(PARTS):
                        w = (w0_lo if hl == "hl" else w0_hi)[:, s * P:(s + 1) * P]
                        y, c = r0 + s // 2, s % 2
                        d = hl0[:, int(hl == "lh"), y:y + rows, c:c + REG]
                        mm = nc.tensor.matmul(acc, w, d, start=(i == 0), stop=(i == len(PARTS) - 1))
                    mm.then_inc(conv0, 1)

            def block1(j, par, k):
                n = 2 * j + par
                if k == 0:
                    pe.wait_ge(w1_ready, n + 1)
                pe.wait_ge(lo1_ready, CH1 * n + k + 1)
                if not (isinstance(n, int) and n == 0 and k < 4):
                    pe.wait_ge(evicted, CH1 * n + k - 3)
                for i, (s, hl) in enumerate(PARTS):
                    w = (w1_lo if hl == "hl" else w1_hi)[par][:, s * P:(s + 1) * P]
                    y, c = k * L1_ROWS + s // 2, s % 2
                    d = (lo1 if hl == "lh" else hi1)[par][:, y:y + L1_ROWS, c:c + OUT]
                    mm = nc.tensor.matmul(ps1[:, k % 4, :], w, d, start=(i == 0), stop=(i == len(PARTS) - 1))
                mm.then_inc(conv1, 1)

            pe.wait_ge(consts_in, 7 * 16)
            group_sums0(0)
            block0(0)
            group_sums1(0)
            group_sums0(1)
            block0(1)

            def step(j, par, one, two):
                n = 2 * j + par
                for k in range(CH1):
                    block1(j, par, k)
                    if k == 2 and one:
                        group_sums1(n + 1)
                    if k == 5 and two:
                        group_sums0(n + 2)
                if two:
                    block0(n + 2)

            step(0, 0, True, True)
            step(0, 1, True, True)
            with pe.Fori(1, loops) as j:
                step(j, 0, True, True)
                step(j, 1, True, True)
            step(loops, 0, True, False)
            step(loops, 1, False, False)


def kernel(x, L0_conv_weight, L0_conv_bias, L1_conv_weight, L1_conv_bias):
    import numpy as np
    import concourse.bacc as bacc
    from concourse.bass_utils import run_bass_kernel_spmd

    x = np.asarray(x)
    B, C, H, W = x.shape
    padded = np.zeros((B, C, H + 2, W + 2), x.dtype)
    padded[:, :, 1:-1, 1:-1] = x
    cells = padded.reshape(B, C, SIDE, 2, SIDE, 2).transpose(0, 3, 5, 1, 2, 4)

    def toeplitz(weight, tap):
        weight = np.asarray(weight)
        big = np.zeros((2, 2, C, 2, 2, 2, 2, C), weight.dtype)
        for a, b, sy, sx, c, d in np.ndindex(2, 2, 2, 2, 2, 2):
            kh, kw = tap(sy, a, c), tap(sx, b, d)
            if 0 <= kh < 3 and 0 <= kw < 3:
                big[a, b, :, sy, sx, c, d, :] = weight[:, :, kh, kw].T
        return big.reshape(P, 4 * P)

    def tap1(s, a, c):
        return 2 * s + a - c

    def tap0(s, a, c):
        return 2 + c - 2 * s - a

    centre = np.zeros((C, C, 3, 3), np.float32)
    centre[np.arange(C), np.arange(C), 1, 1] = 1.0
    channel = np.arange(P) % C
    same_group = (channel[:, None] // 2 == channel[None, :] // 2).astype(np.float32)
    arrays = {
        "x": np.ascontiguousarray(cells).reshape(B, P, CELLS),
        "w0": toeplitz(L0_conv_weight, tap0),
        "w1": toeplitz(L1_conv_weight, tap1),
        "ident": toeplitz(centre, tap1),
        "g0": same_group * np.float32(PAD_K / 8),
        "g1": same_group * np.float32(1 / 8),
        "bias0": np.tile(np.asarray(L0_conv_bias), 4).reshape(P, 1),
        "bias1": np.tile(np.asarray(L1_conv_bias), 4).reshape(P, 1),
    }
    nc = bacc.Bacc("TRN2", target_bir_lowering=False, num_devices=1)
    args = [nc.dram_tensor(name, a.shape, F32, kind="ExternalInput").ap() for name, a in arrays.items()]
    out = nc.dram_tensor("out", (B, P, VALID), F32, kind="ExternalOutput").ap()
    conv_blocks(nc, *args, out)
    r = run_bass_kernel_spmd(nc, [arrays], core_ids=[0])
    got = r.results[0]["out"].reshape(B, 2, 2, C, OUT, OUT)
    return got.transpose(0, 3, 4, 1, 5, 2).reshape(B, C, H, W)
```

```python
from contextlib import ExitStack

import concourse.bass as bass
from concourse import mybir

F32 = mybir.dt.float32
F32R = mybir.dt.float32r
ALU = mybir.AluOpType
ACT = mybir.ActivationFunctionType

P = 128
SIDE = 65
CELLS = SIDE * SIDE
OUT = 64
VALID = OUT * OUT
REG = 34
SRC = SIDE - REG
EPS = 1e-5
FFT_SCALE = 1.0 / 256.0
PAD_K = CELLS / VALID

L0_ROWS = [(0, 12), (12, 11), (23, 11)]
L1_ROWS = 8
CH1 = OUT // L1_ROWS
HD_ROWS = [(0, 9)] + [(9 + 8 * k, 8) for k in range(7)]
REST = [(r0, n, REG, SIDE - REG) for r0, n in L0_ROWS] + [(34, 7, 0, SIDE)] + [
    (41 + 6 * k, 6, 0, SIDE) for k in range(4)]
N0, NR = len(L0_ROWS), len(REST)
SUMS_AT = 3
CONSTS = 6
PARTS = [(s, hl) for s in range(4) for hl in ("hh", "hl", "lh")]


def conv_blocks(nc, x, w0, w1, ident, g, bias0, bias1, out):
    images = x.shape[0]
    with ExitStack() as ctx:
        def sb(name, shape, dt=F32):
            return ctx.enter_context(nc.sbuf_tensor(name, shape, dt))

        def ps(name, shape):
            return ctx.enter_context(nc.psum_tensor(name, shape, F32))

        def sem(name):
            return ctx.enter_context(nc.semaphore(name))

        xs = [sb(f"x_{p}", [P, SIDE, SIDE]) for p in range(2)]
        hi1 = [sb(f"hi1_{p}", [P, SIDE, SIDE], F32R) for p in range(2)]
        lo1 = [sb(f"lo1_{p}", [P, SIDE, SIDE], F32R) for p in range(2)]
        hl0 = sb("hl0", [P, 2, REG + 1, REG + 1], F32R)
        w0_base, w1_base = sb("w0_base", [P, 512]), sb("w1_base", [P, 512])
        identity = sb("identity", [P, 512])
        w_scaled = sb("w_scaled", [P, 512])
        w0_hi, w0_lo = sb("w0_hi", [P, 512], F32R), sb("w0_lo", [P, 512], F32R)
        w1_hi = [sb(f"w1_hi_{p}", [P, 512], F32R) for p in range(2)]
        w1_lo = [sb(f"w1_lo_{p}", [P, 512], F32R) for p in range(2)]
        group = sb("group", [P, P])
        b0, b1 = sb("b0", [P, 1]), sb("b1", [P, 1])
        b0_2, b0_sq = sb("b0_2", [P, 1]), sb("b0_sq", [P, 1])
        bn = [sb(f"bn_{p}", [P, N0 + NR, 6]) for p in range(2)]
        mv = sb("mv", [P, 2])
        mom = sb("mom", [P, 4])
        tmp = sb("tmp", [P, 8])
        neg_mean0 = sb("neg_mean0", [P, 1])
        neg_mean1 = [sb(f"neg_mean1_{p}", [P, 1]) for p in range(2)]
        out_bias = [sb(f"out_bias_{p}", [P, 1]) for p in range(2)]
        var, std, rstd = sb("var", [P, 2]), sb("std", [P, 2]), sb("rstd", [P, 2])
        stage = sb("stage", [P, CH1 // 2, 2 * 512])

        ps1 = ps("ps1", [P, 4, 512])
        ps0 = ps("ps0", [P, N0, 512])
        psg = ps("psg", [P, 4])

        consts_in = sem("consts_in")
        x_top = [sem(f"x_top_{p}") for p in range(2)]
        x_bottom = [sem(f"x_bottom_{p}") for p in range(2)]
        dve_done = sem("dve_done")
        moments, sums = sem("moments"), sem("sums")
        var_ready, std_ready = sem("var_ready"), sem("std_ready")
        mean1 = sem("mean1")
        hi0_ready, operands0, w1_ready = sem("hi0_ready"), sem("operands0"), sem("w1_ready")
        conv0 = sem("conv0")
        hd1_ready, lo1_ready = sem("hd1_ready"), sem("lo1_ready")
        conv1, evicted = sem("conv1"), sem("evicted")
        stored = [sem(f"stored_{k}") for k in range(CH1 // 2)]
        block = ctx.enter_context(nc.Block())

        loops = (images - 2) // 2

        @block.sync
        def _(sp):
            def load(j, par):
                sp.dma_start(xs[par][:, 0:REG, :].rearrange("p y x -> p (y x)"),
                             x[2 * j + par, :, 0:REG * SIDE]).then_inc(x_top[par], 16)
                sp.dma_start(xs[par][:, REG:SIDE, :].rearrange("p y x -> p (y x)"),
                             x[2 * j + par, :, REG * SIDE:CELLS]).then_inc(x_bottom[par], 16)

            def store(j, par):
                for k in range(CH1 // 2):
                    sp.wait_ge(evicted, CH1 * (2 * j + par) + 2 * k + 2)
                    sp.dma_start(out[2 * j + par, :, k * 1024:(k + 1) * 1024], stage[:, k, :]).then_inc(stored[k], 16)

            load(0, 0)
            for dst, src in ((group, g), (b0, bias0), (b1, bias1), (w0_base, w0), (w1_base, w1),
                             (identity, ident)):
                sp.dma_start(dst[:], src).then_inc(consts_in, 16)
            load(0, 1)

            def step(j, par, ahead):
                if ahead:
                    sp.wait_ge(lo1_ready, CH1 * (2 * j + par + 1))
                    load(j + 1, par)
                store(j, par)

            with sp.Fori(0, loops) as j:
                step(j, 0, True)
                step(j, 1, True)
            step(loops, 0, False)
            step(loops, 1, False)
            for k in range(CH1 // 2):
                sp.wait_ge(stored[k], 16 * images)

        @block.vector
        def _(dve):
            SETUP, SOURCE, SUMMED, CHAIN = 3, 4, 9, 12
            CHAIN_OF = {(True, True): CHAIN, (True, False): CHAIN - 2, (False, True): CHAIN - 2}
            count = {"base": 0, "n": 0}

            def begin(base):
                count.update(base=base, n=0)

            def done(ins):
                count["n"] += 1
                ins.then_inc(dve_done, 1)

            def settle():
                dve.wait_ge(dve_done, count["base"] + count["n"])

            def end(steps):
                assert count["n"] == steps, (count, steps)

            def aggregate(par):
                settle()
                nc.vector.memset(tmp[:, 0:1], 0.0)
                done(nc.vector.bn_aggr(mv[:], bn[par][:].rearrange("p k s -> p (k s)")))
                settle()

            def source_stats(j, par, base, last=True):
                begin(base)
                X = xs[par]
                dve.wait_ge(x_top[par], 16 * (j + 1))
                for k, (r0, rows) in enumerate(L0_ROWS):
                    nc.vector.bn_stats(bn[par][:, k, :], X[:, r0:r0 + rows, 0:REG])
                for k, (r0, rows, c0, cols) in enumerate(REST):
                    if r0 == REG:
                        dve.wait_ge(x_bottom[par], 16 * (j + 1))
                    stats = nc.vector.bn_stats(bn[par][:, N0 + k, :], X[:, r0:r0 + rows, c0:c0 + cols])
                done(stats)
                aggregate(par)
                done(nc.vector.tensor_scalar(mom[:, 0:1], mv[:, 0:1], PAD_K, None, ALU.mult))
                done(nc.vector.scalar_tensor_tensor(tmp[:, 0:1], mv[:, 0:1], mv[:, 0:1], mv[:, 1:2], ALU.mult, ALU.add))
                settle()
                square = nc.vector.tensor_scalar(mom[:, 2:3], tmp[:, 0:1], PAD_K, None, ALU.mult)
                if last:
                    square.then_inc(moments, 1)
                end(SOURCE)

            def summed_stats(j, par, base, last=False):
                begin(base)
                n = 2 * j + par
                X = xs[par]
                for k, (r0, rows) in enumerate(L0_ROWS):
                    dve.wait_ge(conv0, N0 * n + k + 1)
                    area = X[:, r0:r0 + rows, 0:REG]
                    done(nc.vector.tensor_tensor(area, area, ps0[:, k, 0:rows * REG].rearrange("p (y x) -> p y x", x=REG),
                                                 ALU.add))
                settle()
                nc.vector.memset(X[0:64, 0:1, 0:REG], 0.0)
                nc.vector.memset(X[0:32, 1:REG, 0:1], 0.0)
                done(nc.vector.memset(X[64:96, 0:REG, 0:1], 0.0))
                settle()
                for k, (r0, rows) in enumerate(L0_ROWS):
                    stats = nc.vector.bn_stats(bn[par][:, k, :], X[:, r0:r0 + rows, 0:REG])
                done(stats)
                aggregate(par)
                done(nc.vector.tensor_scalar(mom[:, 1:2], mv[:, 0:1], PAD_K, b0[:, 0:1], ALU.mult, ALU.add))
                done(nc.vector.scalar_tensor_tensor(tmp[:, 0:1], mv[:, 0:1], mv[:, 0:1], mv[:, 1:2], ALU.mult, ALU.add))
                settle()
                done(nc.vector.tensor_scalar(tmp[:, 1:2], mom[:, 1:2], b0_2[:, 0:1], b0_sq[:, 0:1], ALU.mult,
                                             ALU.subtract))
                settle()
                square = nc.vector.scalar_tensor_tensor(mom[:, 3:4], tmp[:, 0:1], PAD_K, tmp[:, 1:2], ALU.mult, ALU.add)
                if last:
                    square.then_inc(moments, 1)
                end(SUMMED)

            def chain(s, j1, par, j0, base):
                begin(base)
                n = s - 1
                dve.wait_ge(sums, s + 1)
                if j0 is not None:
                    nc.vector.tensor_scalar(neg_mean0[:], psg[:, 0:1], -1.0, None, ALU.mult)
                if j1 is not None:
                    wait_before(evicted, CH1, j1, par)
                    nc.vector.tensor_tensor(neg_mean1[par][:], b0[:], psg[:, 1:2], ALU.subtract)
                    nc.vector.tensor_tensor(out_bias[par][:], b1[:], psg[:, 1:2], ALU.add)
                done(nc.vector.tensor_copy(tmp[:, 0:2], psg[:, 0:2]))
                settle()
                done(nc.vector.tensor_tensor(tmp[:, 2:4], tmp[:, 0:2], tmp[:, 0:2], ALU.mult))
                settle()
                done(nc.vector.tensor_tensor(tmp[:, 4:6], psg[:, 2:4], tmp[:, 2:4], ALU.subtract))
                settle()
                nc.vector.tensor_scalar(var[:], tmp[:, 4:6], EPS, None, ALU.add).then_inc(var_ready, 1)
                if j1 is not None:
                    X = xs[par]
                    for p0, p1, edge in ((0, 64, X[0:64, 0, :]), (64, 128, X[64:128, SIDE - 1, :]),
                                         (0, 32, X[0:32, 1:SIDE, 0]), (64, 96, X[64:96, 0:SIDE - 1, 0]),
                                         (32, 64, X[32:64, 1:SIDE, SIDE - 1]), (96, 128, X[96:128, 0:SIDE - 1, SIDE - 1])):
                        mean = neg_mean1[par][p0:p1, 0:1].broadcast_to([p1 - p0, edge.shape[1]])
                        fill = nc.vector.tensor_scalar(edge, mean, -1.0, None, ALU.mult)
                    fill.then_inc(mean1, 1)
                dve.wait_ge(std_ready, s + 1)
                r = tmp[:, 0:2]
                done(nc.vector.reciprocal(r, std[:]))
                settle()
                done(nc.vector.tensor_tensor(tmp[:, 2:4], r, r, ALU.mult))
                settle()
                done(nc.vector.tensor_tensor(tmp[:, 4:6], tmp[:, 2:4], var[:], ALU.mult))
                settle()
                done(nc.vector.tensor_scalar(tmp[:, 6:8], tmp[:, 4:6], -0.5, 1.5, ALU.mult, ALU.add))
                settle()
                done(nc.vector.tensor_tensor(rstd[:], r, tmp[:, 6:8], ALU.mult))
                settle()
                if j0 is not None:
                    done(nc.vector.tensor_scalar(w0_hi[:], w0_base[:], rstd[:, 0:1], None, ALU.mult))
                if j1 is not None:
                    done(nc.vector.scalar_tensor_tensor(w_scaled[:], w1_base[:], rstd[:, 1:2], identity[:], ALU.mult,
                                                        ALU.add))
                settle()
                if j0 is not None:
                    nc.vector.scalar_tensor_tensor(w0_lo[:], w0_base[:], rstd[:, 0:1], w0_hi[:].bitcast(F32), ALU.mult,
                                                   ALU.subtract)
                if j1 is not None:
                    wait_before(conv1, CH1, j1, par)
                    done(nc.vector.tensor_copy(w1_hi[par][:], w_scaled[:]))
                if j0 is not None:
                    X = xs[1 - par]
                    dve.wait_ge(hi0_ready, s + 1)
                    done(nc.vector.scalar_tensor_tensor(hl0[:, 1, 0:REG, 0:REG], X[:, SRC:SIDE, SRC:SIDE],
                                                        neg_mean0[:, 0:1], hl0[:, 0, 0:REG, 0:REG].bitcast(F32), ALU.add,
                                                        ALU.subtract))
                    settle()
                    z = hl0[:].bitcast(F32)
                    nc.vector.memset(z[64:128, :, REG - 1:REG, 0:REG], 0.0)
                    nc.vector.memset(z[32:64, :, 0:REG, REG - 1:REG], 0.0)
                    nc.vector.memset(z[96:128, :, 0:REG - 1, REG - 1:REG], 0.0).then_inc(operands0, 1)
                if j1 is not None:
                    settle()
                    nc.vector.tensor_tensor(w1_lo[par][:], w_scaled[:], w1_hi[par][:].bitcast(F32),
                                            ALU.subtract).then_inc(w1_ready, 1)
                end(CHAIN_OF[j0 is not None, j1 is not None])

            def wait_before(s, per, j, par):
                if not (isinstance(j, int) and j == 0):
                    dve.wait_ge(s, per * (2 * j + par - 1))

            nc.vector.memset(hl0[:].bitcast(F32), 0.0)
            nc.vector.memset(mom[:], 0.0)
            source_stats(0, 0, 0)
            begin(SOURCE)
            dve.wait_ge(consts_in, CONSTS * 16)
            done(nc.vector.tensor_scalar(w0_base[:], w0_base[:], FFT_SCALE, None, ALU.mult))
            done(nc.vector.tensor_scalar(b0_2[:], b0[:], 2.0, None, ALU.mult))
            done(nc.vector.tensor_tensor(b0_sq[:], b0[:], b0[:], ALU.mult))
            settle()
            at = SOURCE + SETUP
            chain(0, None, 1, 0, at)
            at += CHAIN_OF[True, False]
            source_stats(0, 1, at, last=False)
            at += SOURCE
            summed_stats(0, 0, at, last=True)
            at += SUMMED
            chain(1, 0, 0, 0, at)
            first = at + CHAIN

            def step(j, par, two):
                n = 2 * j + par
                at = first + (SUMMED + SOURCE + CHAIN) * n
                summed_stats(j + par, 1 - par, at, last=not two)
                if two:
                    source_stats(j + 1, par, at + SUMMED)
                chain(n + 2, j + par, 1 - par, j + 1 if two else None, at + SUMMED + (SOURCE if two else 0))

            step(0, 0, True)
            with dve.Fori(0, loops - 1) as j:
                step(j, 1, True)
                step(j + 1, 0, True)
            step(loops - 1, 1, True)
            step(loops, 0, False)

        @block.scalar
        def _(act):
            def root(s):
                act.wait_ge(var_ready, s + 1)
                nc.scalar.activation(std[:], var[:], ACT.Sqrt).then_inc(std_ready, 1)

            def high0(j, par):
                nc.scalar.activation(hl0[:, 0, 0:REG, 0:REG], xs[par][:, SRC:SIDE, SRC:SIDE], ACT.Identity,
                                     bias=neg_mean0[:, 0:1]).then_inc(hi0_ready, 1)

            def high1(j, par, k):
                n = 2 * j + par
                if k == 0:
                    act.wait_ge(mean1, n + 1)
                    if not (isinstance(j, int) and j == 0):
                        act.wait_ge(conv1, CH1 * (n - 1))
                r0, rows = HD_ROWS[k]
                src = xs[par][:, r0:r0 + rows, :]
                nc.scalar.activation(hi1[par][:, r0:r0 + rows, :], src, ACT.Identity, bias=neg_mean1[par][:, 0:1])
                nc.scalar.activation(src, src, ACT.Identity, bias=neg_mean1[par][:, 0:1]).then_inc(hd1_ready, 1)

            def evict(j, par, k):
                n = 2 * j + par
                act.wait_ge(conv1, CH1 * n + k + 1)
                if k % 2 == 0 and not (isinstance(n, int) and n == 0):
                    act.wait_ge(stored[k // 2], 16 * n)
                nc.scalar.activation(stage[:, k // 2, 512 * (k % 2):512 * (k % 2) + 512], ps1[:, k % 4, :], ACT.Identity,
                                     bias=out_bias[par][:, 0:1]).then_inc(evicted, 1)

            root(0)
            high0(0, 0)
            root(1)
            high0(0, 1)
            for k in range(CH1):
                high1(0, 0, k)

            def step(j, par, one, two):
                for k in range(CH1):
                    evict(j, par, k)
                    if k == SUMS_AT and one:
                        root(2 * j + par + 2)
                    if k == SUMS_AT + 1 and two:
                        high0(j + 1, par)
                    if k >= SUMS_AT and one:
                        for part in (2 * (k - SUMS_AT), 2 * (k - SUMS_AT) + 1):
                            if part < CH1:
                                high1(j + par, 1 - par, part)

            step(0, 0, True, True)
            with act.Fori(0, loops - 1) as j:
                step(j, 1, True, True)
                step(j + 1, 0, True, True)
            step(loops - 1, 1, True, True)
            step(loops, 0, True, False)
            step(loops, 1, False, False)

        @block.gpsimd
        def _(pool):
            def low1(j, par):
                n = 2 * j + par
                for k, (r0, rows) in enumerate(HD_ROWS):
                    pool.wait_ge(hd1_ready, CH1 * n + k + 1)
                    if k == 0 and not (isinstance(j, int) and j == 0):
                        pool.wait_ge(conv1, CH1 * (n - 1))
                    part = slice(r0, r0 + rows)
                    nc.gpsimd.tensor_tensor(lo1[par][:, part, :], xs[par][:, part, :],
                                            hi1[par][:, part, :].bitcast(F32), ALU.subtract).then_inc(lo1_ready, 1)

            low1(0, 0)
            low1(0, 1)
            with pool.Fori(1, images // 2) as j:
                low1(j, 0)
                low1(j, 1)

        @block.tensor
        def _(pe):
            def group_sums(s):
                pe.wait_ge(moments, s + 1)
                nc.tensor.matmul(psg[:], group[:], mom[:], start=True, stop=True).then_inc(sums, 1)

            def block0(n):
                pe.wait_ge(operands0, n + 1)
                for k, (r0, rows) in enumerate(L0_ROWS):
                    acc = ps0[:, k, 0:rows * REG].rearrange("p (y x) -> p y x", x=REG)
                    for i, (s, hl) in enumerate(PARTS):
                        w = (w0_lo if hl == "hl" else w0_hi)[:, s * P:(s + 1) * P]
                        y, c = r0 + s // 2, s % 2
                        d = hl0[:, int(hl == "lh"), y:y + rows, c:c + REG]
                        mm = nc.tensor.matmul(acc, w, d, start=(i == 0), stop=(i == len(PARTS) - 1))
                    mm.then_inc(conv0, 1)

            def block1(j, par, k):
                n = 2 * j + par
                if k == 0:
                    pe.wait_ge(w1_ready, n + 1)
                pe.wait_ge(lo1_ready, CH1 * n + k + 1)
                if not (isinstance(n, int) and n == 0 and k < 4):
                    pe.wait_ge(evicted, CH1 * n + k - 3)
                for i, (s, hl) in enumerate(PARTS):
                    w = (w1_lo if hl == "hl" else w1_hi)[par][:, s * P:(s + 1) * P]
                    y, c = k * L1_ROWS + s // 2, s % 2
                    d = (lo1 if hl == "lh" else hi1)[par][:, y:y + L1_ROWS, c:c + OUT]
                    mm = nc.tensor.matmul(ps1[:, k % 4, :], w, d, start=(i == 0), stop=(i == len(PARTS) - 1))
                mm.then_inc(conv1, 1)

            pe.wait_ge(consts_in, CONSTS * 16)
            group_sums(0)
            block0(0)
            group_sums(1)
            block0(1)

            def step(j, par, one, two):
                n = 2 * j + par
                for k in range(CH1):
                    block1(j, par, k)
                    if k == SUMS_AT and one:
                        group_sums(n + 2)
                if two:
                    block0(n + 2)

            step(0, 0, True, True)
            with pe.Fori(0, loops - 1) as j:
                step(j, 1, True, True)
                step(j + 1, 0, True, True)
            step(loops - 1, 1, True, True)
            step(loops, 0, True, False)
            step(loops, 1, False, False)


def kernel(x, L0_conv_weight, L0_conv_bias, L1_conv_weight, L1_conv_bias):
    import numpy as np
    import concourse.bacc as bacc
    from concourse.bass_utils import run_bass_kernel_spmd

    x = np.asarray(x)
    B, C, H, W = x.shape
    padded = np.zeros((B, C, H + 2, W + 2), x.dtype)
    padded[:, :, 1:-1, 1:-1] = x
    cells = padded.reshape(B, C, SIDE, 2, SIDE, 2).transpose(0, 3, 5, 1, 2, 4)

    def toeplitz(weight, tap):
        weight = np.asarray(weight)
        big = np.zeros((2, 2, C, 2, 2, 2, 2, C), weight.dtype)
        for a, b, sy, sx, c, d in np.ndindex(2, 2, 2, 2, 2, 2):
            kh, kw = tap(sy, a, c), tap(sx, b, d)
            if 0 <= kh < 3 and 0 <= kw < 3:
                big[a, b, :, sy, sx, c, d, :] = weight[:, :, kh, kw].T
        return big.reshape(P, 4 * P)

    def tap1(s, a, c):
        return 2 * s + a - c

    def tap0(s, a, c):
        return 2 + c - 2 * s - a

    centre = np.zeros((C, C, 3, 3), np.float32)
    centre[np.arange(C), np.arange(C), 1, 1] = 1.0
    channel = np.arange(P) % C
    same_group = (channel[:, None] // 2 == channel[None, :] // 2).astype(np.float32)
    arrays = {
        "x": np.ascontiguousarray(cells).reshape(B, P, CELLS),
        "w0": toeplitz(L0_conv_weight, tap0),
        "w1": toeplitz(L1_conv_weight, tap1),
        "ident": toeplitz(centre, tap1),
        "g": same_group / np.float32(8),
        "bias0": np.tile(np.asarray(L0_conv_bias), 4).reshape(P, 1),
        "bias1": np.tile(np.asarray(L1_conv_bias), 4).reshape(P, 1),
    }
    nc = bacc.Bacc("TRN2", target_bir_lowering=False, num_devices=1)
    args = [nc.dram_tensor(name, a.shape, F32, kind="ExternalInput").ap() for name, a in arrays.items()]
    out = nc.dram_tensor("out", (B, P, VALID), F32, kind="ExternalOutput").ap()
    conv_blocks(nc, *args, out)
    r = run_bass_kernel_spmd(nc, [arrays], core_ids=[0])
    got = r.results[0]["out"].reshape(B, 2, 2, C, OUT, OUT)
    return got.transpose(0, 3, 4, 1, 5, 2).reshape(B, C, H, W)
```

```python
from contextlib import ExitStack

import concourse.bass as bass
from concourse import mybir

F32 = mybir.dt.float32
F32R = mybir.dt.float32r
ALU = mybir.AluOpType
ACT = mybir.ActivationFunctionType

P = 128
SIDE = 65
CELLS = SIDE * SIDE
OUT = 64
VALID = OUT * OUT
REG = 34
SRC = SIDE - REG
EPS = 1e-5
FFT_SCALE = 1.0 / 256.0
PAD_K = CELLS / VALID

L0_ROWS = [(0, 12), (12, 11), (23, 11)]
L1_ROWS = 8
CH1 = OUT // L1_ROWS
HD_ROWS = [(0, 9)] + [(9 + 8 * k, 8) for k in range(7)]
PIECES = [(0, 12), (12, 34), (34, 48), (48, SIDE)]
STATS = [(0, 12, 0, REG, 0), (12, 11, 0, REG, 1), (23, 11, 0, REG, 1),
         (0, 12, REG, SIDE - REG, 0), (12, 11, REG, SIDE - REG, 1), (23, 11, REG, SIDE - REG, 1),
         (34, 7, 0, SIDE, 2), (41, 7, 0, SIDE, 2), (48, 6, 0, SIDE, 3), (54, 6, 0, SIDE, 3), (60, 5, 0, SIDE, 3)]
ORDER = sorted(range(len(STATS)), key=lambda k: STATS[k][4])
N0 = len(L0_ROWS)
EARLY = 5
EARLY2 = 6
FIRST_AT = 1
ROOT_AT = 6
SUMS_AT = 4
CONSTS0, CONSTS1 = 4, 2
WARM = (32, 12, 14, 13)
PRODUCTS = ("hh", "hl", "lh")


def conv_blocks(nc, x, w0, w1, ident, g, bias0, bias1, out):
    images = x.shape[0]
    with ExitStack() as ctx:
        def sb(name, shape, dt=F32):
            return ctx.enter_context(nc.sbuf_tensor(name, shape, dt))

        def ps(name, shape):
            return ctx.enter_context(nc.psum_tensor(name, shape, F32))

        def sem(name):
            return ctx.enter_context(nc.semaphore(name))

        xs = [sb(f"x_{p}", [P, SIDE, SIDE]) for p in range(2)]
        hi1 = [sb(f"hi1_{p}", [P, SIDE, SIDE], F32R) for p in range(2)]
        lo1 = [sb(f"lo1_{p}", [P, SIDE, SIDE], F32R) for p in range(2)]
        hl0 = sb("hl0", [P, 2, REG + 1, REG + 1], F32R)
        w0_base, w1_base = sb("w0_base", [P, 512]), sb("w1_base", [P, 512])
        identity = sb("identity", [P, 512])
        w_scaled = sb("w_scaled", [P, 512])
        w0_hi, w0_lo = sb("w0_hi", [P, 512], F32R), sb("w0_lo", [P, 512], F32R)
        w1_hi = [sb(f"w1_hi_{p}", [P, 512], F32R) for p in range(2)]
        w1_lo = [sb(f"w1_lo_{p}", [P, 512], F32R) for p in range(2)]
        group = sb("group", [P, P])
        b0, b1 = sb("b0", [P, 1]), sb("b1", [P, 1])
        b0_2, b0_sq = sb("b0_2", [P, 1]), sb("b0_sq", [P, 1])
        bn = [sb(f"bn_{p}", [P, len(STATS), 6]) for p in range(2)]
        mv = sb("mv", [P, 2])
        mom = sb("mom", [P, 4])
        tmp = sb("tmp", [P, 8])
        neg_mean0 = sb("neg_mean0", [P, 1])
        neg_mean1 = [sb(f"neg_mean1_{p}", [P, 1]) for p in range(2)]
        out_bias = [sb(f"out_bias_{p}", [P, 1]) for p in range(2)]
        var, std, rstd = sb("var", [P, 2]), sb("std", [P, 2]), sb("rstd", [P, 2])
        zeros = sb("zeros", [P, 512], mybir.dt.bfloat16)
        stage = sb("stage", [P, CH1 // 2, 2 * 512])

        ps1 = ps("ps1", [P, 4, 512])
        ps0 = ps("ps0", [P, N0, 512])
        psg = ps("psg", [P, 4])

        consts0_in, consts1_in = sem("consts0_in"), sem("consts1_in")
        zeros_ready = sem("zeros_ready")
        x_in = [[sem(f"x_in_{p}_{q}") for q in range(len(PIECES))] for p in range(2)]
        dve_done = sem("dve_done")
        moments, sums = sem("moments"), sem("sums")
        var_ready, std_ready = sem("var_ready"), sem("std_ready")
        mean1 = sem("mean1")
        hi0_ready, operands0, w1_ready = sem("hi0_ready"), sem("operands0"), sem("w1_ready")
        conv0 = sem("conv0")
        hd1_ready, lo1_ready = sem("hd1_ready"), sem("lo1_ready")
        conv1, evicted = sem("conv1"), sem("evicted")
        stored = [sem(f"stored_{k}") for k in range(CH1 // 2)]
        block = ctx.enter_context(nc.Block())

        loops = (images - 2) // 2

        def sums_at(j, par):
            return SUMS_AT + int(isinstance(j, int) and 2 * j + par == 0)

        @block.sync
        def _(sp):
            def load(j, par, behind=False, pieces=range(len(PIECES))):
                for q in pieces:
                    r0, r1 = PIECES[q]
                    if behind:
                        split = 1 + min(k for k, (first, rows) in enumerate(HD_ROWS) if first + rows >= r1)
                        sp.wait_ge(lo1_ready, CH1 * (2 * j + par - 2) + split)
                    sp.dma_start(xs[par][:, r0:r1, :].rearrange("p y x -> p (y x)"),
                                 x[2 * j + par, :, r0 * SIDE:r1 * SIDE]).then_inc(x_in[par][q], 16)

            def store(j, par, k, c0, c1):
                sp.wait_ge(evicted, CH1 * (2 * j + par) + 2 * k + c1)
                sp.dma_start(out[2 * j + par, :, (2 * k + c0) * 512:(2 * k + c1) * 512],
                             stage[:, k, c0 * 512:c1 * 512]).then_inc(stored[k], 16)

            load(0, 0)
            for dst, src in ((group, g), (b0, bias0), (b1, bias1), (w0_base, w0)):
                sp.dma_start(dst[:], src).then_inc(consts0_in, 16)
            load(0, 1)
            for dst, src in ((w1_base, w1), (identity, ident)):
                sp.dma_start(dst[:], src).then_inc(consts1_in, 16)
            load(1, 0, behind=True)

            def step(j, par, ahead, last=False):
                for k in range(CH1 // 2 - 1):
                    store(j, par, k, 0, 2)
                if ahead:
                    load(j + 1 + par, 1 - par, behind=True, pieces=[0])
                if last:
                    store(j, par, CH1 // 2 - 1, 0, 1)
                    store(j, par, CH1 // 2 - 1, 1, 2)
                else:
                    store(j, par, CH1 // 2 - 1, 0, 2)
                if ahead:
                    load(j + 1 + par, 1 - par, behind=True, pieces=range(1, len(PIECES)))

            with sp.Fori(0, loops - 1) as j:
                step(j, 0, True)
                step(j, 1, True)
            step(loops - 1, 0, True)
            step(loops - 1, 1, False)
            step(loops, 0, False)
            step(loops, 1, False, last=True)
            for k in range(CH1 // 2):
                sp.wait_ge(stored[k], 16 * (images + int(k == CH1 // 2 - 1)))

        @block.vector
        def _(dve):
            SETUP, SOURCE, SUMMED, CHAIN = 3, 4, 9, 11
            CHAIN_OF = {(True, True): CHAIN, (True, False): CHAIN - 2, (False, True): CHAIN - 2}
            count = {"base": 0, "n": 0}

            def begin(base):
                count.update(base=base, n=0)

            def done(ins):
                count["n"] += 1
                ins.then_inc(dve_done, 1)

            def settle():
                dve.wait_ge(dve_done, count["base"] + count["n"])

            def end(steps):
                assert count["n"] == steps, (count, steps)

            def aggregate(par):
                settle()
                nc.vector.memset(tmp[:, 0:1], 0.0)
                done(nc.vector.bn_aggr(mv[:], bn[par][:].rearrange("p k s -> p (k s)")))
                settle()

            def source_stats(j, par, which):
                X = xs[par]
                seen = -1
                for k in which:
                    r0, rows, c0, cols, piece = STATS[k]
                    if piece > seen:
                        dve.wait_ge(x_in[par][piece], 16 * (j + 1))
                        seen = piece
                    stats = nc.vector.bn_stats(bn[par][:, k, :], X[:, r0:r0 + rows, c0:c0 + cols])
                return stats

            def source_moments(j, par, base, which=ORDER):
                begin(base)
                done(source_stats(j, par, which))
                aggregate(par)
                done(nc.vector.tensor_scalar(mom[:, 0:1], mv[:, 0:1], PAD_K, None, ALU.mult))
                done(nc.vector.scalar_tensor_tensor(tmp[:, 0:1], mv[:, 0:1], mv[:, 0:1], mv[:, 1:2], ALU.mult, ALU.add))
                settle()
                nc.vector.tensor_scalar(mom[:, 2:3], tmp[:, 0:1], PAD_K, None, ALU.mult).then_inc(moments, 1)
                end(SOURCE)

            def summed_moments(j, par, base, last=False):
                begin(base)
                n = 2 * j + par
                X = xs[par]
                for k, (r0, rows) in enumerate(L0_ROWS):
                    dve.wait_ge(conv0, N0 * n + k + 1)
                    area = X[:, r0:r0 + rows, 0:REG]
                    done(nc.vector.tensor_tensor(area, area, ps0[:, k, 0:rows * REG].rearrange("p (y x) -> p y x", x=REG),
                                                 ALU.add))
                settle()
                nc.vector.memset(X[0:64, 0:1, 0:REG], 0.0)
                nc.vector.memset(X[0:32, 1:REG, 0:1], 0.0)
                done(nc.vector.memset(X[64:96, 0:REG, 0:1], 0.0))
                settle()
                for k, (r0, rows) in enumerate(L0_ROWS):
                    stats = nc.vector.bn_stats(bn[par][:, k, :], X[:, r0:r0 + rows, 0:REG])
                done(stats)
                aggregate(par)
                done(nc.vector.tensor_scalar(mom[:, 1:2], mv[:, 0:1], PAD_K, b0[:, 0:1], ALU.mult, ALU.add))
                done(nc.vector.scalar_tensor_tensor(tmp[:, 0:1], mv[:, 0:1], mv[:, 0:1], mv[:, 1:2], ALU.mult, ALU.add))
                settle()
                done(nc.vector.tensor_scalar(tmp[:, 1:2], mom[:, 1:2], b0_2[:, 0:1], b0_sq[:, 0:1], ALU.mult,
                                             ALU.subtract))
                settle()
                square = nc.vector.scalar_tensor_tensor(mom[:, 3:4], tmp[:, 0:1], PAD_K, tmp[:, 1:2], ALU.mult, ALU.add)
                if last:
                    square.then_inc(moments, 1)
                end(SUMMED)

            def pad(par, first, end):
                X = xs[par]
                edges = ((0, 64, X[0:64, 0, :]), (64, 128, X[64:128, SIDE - 1, :]),
                         (0, 32, X[0:32, 1:SIDE, 0]), (64, 96, X[64:96, 0:SIDE - 1, 0]),
                         (32, 64, X[32:64, 1:SIDE, SIDE - 1]), (96, 128, X[96:128, 0:SIDE - 1, SIDE - 1]))
                for p0, p1, edge in edges[first:end]:
                    mean = neg_mean1[par][p0:p1, 0:1].broadcast_to([p1 - p0, edge.shape[1]])
                    fill = nc.vector.tensor_scalar(edge, mean, -1.0, None, ALU.mult)
                return fill

            def chain(s, one, zero, base):
                begin(base)
                if one:
                    j1, par = one
                    n1 = 2 * j1 + par
                if zero:
                    j0, par0 = zero
                    n0 = 2 * j0 + par0
                dve.wait_ge(sums, s + 1)
                if one:
                    wait_before(evicted, CH1, j1, par)
                    done(nc.vector.tensor_tensor(neg_mean1[par][:], b0[:], psg[:, 1:2], ALU.subtract))
                done(nc.vector.tensor_copy(tmp[:, 0:2], psg[:, 0:2]))
                if zero:
                    nc.vector.tensor_scalar(neg_mean0[:], psg[:, 0:1], -1.0, None, ALU.mult)
                settle()
                done(nc.vector.tensor_tensor(tmp[:, 2:4], tmp[:, 0:2], tmp[:, 0:2], ALU.mult))
                if one:
                    pad(par, 0, 1)
                settle()
                done(nc.vector.tensor_tensor(tmp[:, 4:6], psg[:, 2:4], tmp[:, 2:4], ALU.subtract))
                if one:
                    pad(par, 1, 2)
                settle()
                nc.vector.tensor_scalar(var[:], tmp[:, 4:6], 0.0, EPS, ALU.max, ALU.add).then_inc(var_ready, 1)
                if one:
                    nc.vector.tensor_tensor(out_bias[par][:], b1[:], psg[:, 1:2], ALU.add)
                    pad(par, 2, 6).then_inc(mean1, 1)
                dve.wait_ge(std_ready, s + 1)
                r = tmp[:, 0:2]
                done(nc.vector.reciprocal(r, std[:]))
                settle()
                done(nc.vector.scalar_tensor_tensor(tmp[:, 2:4], r, -0.5, r, ALU.mult, ALU.mult))
                settle()
                done(nc.vector.tensor_tensor(tmp[:, 4:6], tmp[:, 2:4], var[:], ALU.mult))
                settle()
                done(nc.vector.scalar_tensor_tensor(rstd[:], tmp[:, 4:6], 1.5, r, ALU.add, ALU.mult))
                settle()

                def operands_of_block0():
                    X = xs[par0]
                    z = hl0[:].bitcast(F32)

                    def zero_padding(part):
                        nc.vector.memset(z[64:128, part, REG - 1:REG, 0:REG], 0.0)
                        nc.vector.memset(z[32:64, part, 0:REG, REG - 1:REG], 0.0)
                        return nc.vector.memset(z[96:128, part, 0:REG - 1, REG - 1:REG], 0.0)

                    done(nc.vector.tensor_scalar(w0_hi[:], w0_base[:], rstd[:, 0:1], None, ALU.mult))
                    dve.wait_ge(hi0_ready, n0 + 1)
                    zero_padding(0).then_inc(operands0, 1)
                    settle()
                    nc.vector.scalar_tensor_tensor(w0_lo[:], w0_base[:], rstd[:, 0:1], w0_hi[:].bitcast(F32), ALU.mult,
                                                   ALU.subtract).then_inc(operands0, 1)
                    dve.wait_ge(operands0, 3 * n0 + 1)
                    done(nc.vector.scalar_tensor_tensor(hl0[:, 1, 0:REG, 0:REG], X[:, SRC:SIDE, SRC:SIDE],
                                                        neg_mean0[:, 0:1], hl0[:, 0, 0:REG, 0:REG].bitcast(F32), ALU.add,
                                                        ALU.subtract))
                    settle()
                    zero_padding(1).then_inc(operands0, 1)

                def weights_of_block1():
                    wait_before(conv1, CH1, j1, par)
                    nc.vector.scalar_tensor_tensor(w1_hi[par][:], w1_base[:], rstd[:, 1:2], identity[:], ALU.mult,
                                                   ALU.add).then_inc(w1_ready, 1)
                    done(nc.vector.scalar_tensor_tensor(w_scaled[:], w1_base[:], rstd[:, 1:2], identity[:], ALU.mult,
                                                        ALU.add))
                    settle()
                    dve.wait_ge(w1_ready, 2 * n1 + 1)
                    nc.vector.tensor_tensor(w1_lo[par][:], w_scaled[:], w1_hi[par][:].bitcast(F32),
                                            ALU.subtract).then_inc(w1_ready, 1)

                if zero:
                    operands_of_block0()
                if one:
                    weights_of_block1()
                end(CHAIN_OF[bool(zero), bool(one)])

            def wait_before(s, per, j, par):
                if not (isinstance(j, int) and j == 0):
                    dve.wait_ge(s, per * (2 * j + par - 1))

            nc.vector.memset(zeros[:], 0.0).then_inc(zeros_ready, 1)
            nc.vector.memset(hl0[:].bitcast(F32), 0.0)
            nc.vector.memset(mom[:], 0.0)
            source_moments(0, 0, 0)
            begin(SOURCE)
            dve.wait_ge(consts0_in, CONSTS0 * 16)
            done(nc.vector.tensor_scalar(w0_base[:], w0_base[:], FFT_SCALE, None, ALU.mult))
            done(nc.vector.tensor_scalar(b0_2[:], b0[:], 2.0, None, ALU.mult))
            done(nc.vector.tensor_tensor(b0_sq[:], b0[:], b0[:], ALU.mult))
            settle()
            at = SOURCE + SETUP
            chain(0, None, (0, 0), at)
            at += CHAIN_OF[True, False]
            source_stats(0, 1, ORDER[:EARLY])
            summed_moments(0, 0, at, last=True)
            at += SUMMED
            dve.wait_ge(consts1_in, CONSTS1 * 16)
            chain(1, (0, 0), None, at)
            at += CHAIN_OF[False, True]
            source_moments(0, 1, at, ORDER[EARLY:])
            at += SOURCE
            chain(2, None, (0, 1), at)
            source_stats(1, 0, ORDER[:EARLY2])
            first = at + CHAIN_OF[True, False]

            def step(j, par, two):
                n = 2 * j + par
                at = first + (SUMMED + SOURCE + CHAIN) * n
                summed_moments(j + par, 1 - par, at, last=not two)
                if two:
                    started = EARLY2 if isinstance(n, int) and n == 0 else 0
                    source_moments(j + 1, par, at + SUMMED, ORDER[started:])
                chain(n + 3, (j + par, 1 - par), (j + 1, par) if two else None, at + SUMMED + (SOURCE if two else 0))

            step(0, 0, True)
            with dve.Fori(0, loops - 1) as j:
                step(j, 1, True)
                step(j + 1, 0, True)
            step(loops - 1, 1, True)
            step(loops, 0, False)

        @block.scalar
        def _(act):
            def root(s):
                act.wait_ge(var_ready, s + 1)
                nc.scalar.activation(std[:], var[:], ACT.Sqrt).then_inc(std_ready, 1)

            def high0(j, par):
                nc.scalar.activation(hl0[:, 0, 0:REG, 0:REG], xs[par][:, SRC:SIDE, SRC:SIDE], ACT.Identity,
                                     bias=neg_mean0[:, 0:1]).then_inc(hi0_ready, 1)

            def high1(j, par, k):
                n = 2 * j + par
                if k == 0:
                    act.wait_ge(mean1, n + 1)
                    if not (isinstance(j, int) and j == 0):
                        act.wait_ge(conv1, CH1 * (n - 1))
                r0, rows = HD_ROWS[k]
                src = xs[par][:, r0:r0 + rows, :]
                nc.scalar.activation(hi1[par][:, r0:r0 + rows, :], src, ACT.Identity, bias=neg_mean1[par][:, 0:1])
                nc.scalar.activation(src, src, ACT.Identity, bias=neg_mean1[par][:, 0:1]).then_inc(hd1_ready, 1)

            def evict(j, par, k):
                n = 2 * j + par
                act.wait_ge(conv1, CH1 * n + k + 1)
                if k % 2 == 0 and not (isinstance(n, int) and n == 0):
                    act.wait_ge(stored[k // 2], 16 * n)
                nc.scalar.activation(stage[:, k // 2, 512 * (k % 2):512 * (k % 2) + 512], ps1[:, k % 4, :], ACT.Identity,
                                     bias=out_bias[par][:, 0:1]).then_inc(evicted, 1)

            root(0)
            high0(0, 0)
            root(1)
            for k in range(CH1):
                if k == ROOT_AT:
                    root(2)
                    high0(0, 1)
                high1(0, 0, k)

            def step(j, par, one, two):
                at = sums_at(j, par)
                for k in range(CH1):
                    evict(j, par, k)
                    if k == at and one:
                        root(2 * j + par + 3)
                    if k >= at and one:
                        for part in range(CH1 * (k - at) // (CH1 - at), CH1 * (k + 1 - at) // (CH1 - at)):
                            high1(j + par, 1 - par, part)
                            if part == 0 and two:
                                high0(j + 1, par)

            step(0, 0, True, True)
            with act.Fori(0, loops - 1) as j:
                step(j, 1, True, True)
                step(j + 1, 0, True, True)
            step(loops - 1, 1, True, True)
            step(loops, 0, True, False)
            step(loops, 1, False, False)

        @block.gpsimd
        def _(pool):
            def low1(j, par):
                n = 2 * j + par
                for k, (r0, rows) in enumerate(HD_ROWS):
                    pool.wait_ge(hd1_ready, CH1 * n + k + 1)
                    if k == 0 and not (isinstance(j, int) and j == 0):
                        pool.wait_ge(conv1, CH1 * (n - 1))
                    part = slice(r0, r0 + rows)
                    nc.gpsimd.tensor_tensor(lo1[par][:, part, :], xs[par][:, part, :],
                                            hi1[par][:, part, :].bitcast(F32), ALU.subtract).then_inc(lo1_ready, 1)

            low1(0, 0)
            low1(0, 1)
            with pool.Fori(1, images // 2) as j:
                low1(j, 0)
                low1(j, 1)

        @block.tensor
        def _(pe):
            def group_sums(s):
                pe.wait_ge(moments, s + 1)
                nc.tensor.matmul(psg[:], group[:], mom[:], start=True, stop=True).then_inc(sums, 1)

            def block0(n):
                for hl in PRODUCTS:
                    pe.wait_ge(operands0, 3 * n + {"hh": 1, "hl": 2, "lh": 3}[hl])
                    for k, (r0, rows) in enumerate(L0_ROWS):
                        acc = ps0[:, k, 0:rows * REG].rearrange("p (y x) -> p y x", x=REG)
                        for s in range(4):
                            w = (w0_lo if hl == "hl" else w0_hi)[:, s * P:(s + 1) * P]
                            y, c = r0 + s // 2, s % 2
                            d = hl0[:, int(hl == "lh"), y:y + rows, c:c + REG]
                            mm = nc.tensor.matmul(acc, w, d, start=(hl == "hh" and s == 0), stop=(hl == "lh" and s == 3))
                        if hl == "lh":
                            mm.then_inc(conv0, 1)

            def block1(j, par, k):
                n = 2 * j + par
                if not (isinstance(n, int) and n == 0 and k < 4):
                    pe.wait_ge(evicted, CH1 * n + k - 3)
                for hl in PRODUCTS:
                    if hl == "hh":
                        pe.wait_ge(hd1_ready, CH1 * n + k + 1)
                    if hl == "lh":
                        pe.wait_ge(lo1_ready, CH1 * n + k + 1)
                    elif k == 0:
                        pe.wait_ge(w1_ready, 2 * n + {"hh": 1, "hl": 2}[hl])
                    for s in range(4):
                        w = (w1_lo if hl == "hl" else w1_hi)[par][:, s * P:(s + 1) * P]
                        y, c = k * L1_ROWS + s // 2, s % 2
                        d = (lo1 if hl == "lh" else hi1)[par][:, y:y + L1_ROWS, c:c + OUT]
                        mm = nc.tensor.matmul(ps1[:, k % 4, :], w, d, start=(hl == "hh" and s == 0),
                                              stop=(hl == "lh" and s == 3))
                mm.then_inc(conv1, 1)

            def keep_warm(products):
                for _ in range(products):
                    nc.tensor.matmul(ps1[:, 3, :], zeros[:, 0:P], zeros[:], start=True, stop=True)

            pe.wait_ge(zeros_ready, 1)
            keep_warm(WARM[0])
            pe.wait_ge(consts0_in, CONSTS0 * 16)
            group_sums(0)
            keep_warm(WARM[1])
            block0(0)
            keep_warm(WARM[2])
            group_sums(1)
            keep_warm(WARM[3])

            def step(j, par, one, two):
                n = 2 * j + par
                for k in range(CH1):
                    block1(j, par, k)
                    if k == FIRST_AT and isinstance(n, int) and n == 0:
                        group_sums(2)
                    if k == FIRST_AT + 1 and isinstance(n, int) and n == 0:
                        block0(1)
                    if k == sums_at(j, par) and one:
                        group_sums(n + 3)
                if two:
                    block0(n + 2)

            step(0, 0, True, True)
            with pe.Fori(0, loops - 1) as j:
                step(j, 1, True, True)
                step(j + 1, 0, True, True)
            step(loops - 1, 1, True, True)
            step(loops, 0, True, False)
            step(loops, 1, False, False)


def kernel(x, L0_conv_weight, L0_conv_bias, L1_conv_weight, L1_conv_bias):
    import numpy as np
    import concourse.bacc as bacc
    from concourse.bass_utils import run_bass_kernel_spmd

    x = np.asarray(x)
    B, C, H, W = x.shape
    padded = np.zeros((B, C, H + 2, W + 2), x.dtype)
    padded[:, :, 1:-1, 1:-1] = x
    cells = padded.reshape(B, C, SIDE, 2, SIDE, 2).transpose(0, 3, 5, 1, 2, 4)

    def toeplitz(weight, tap):
        weight = np.asarray(weight)
        big = np.zeros((2, 2, C, 2, 2, 2, 2, C), weight.dtype)
        for a, b, sy, sx, c, d in np.ndindex(2, 2, 2, 2, 2, 2):
            kh, kw = tap(sy, a, c), tap(sx, b, d)
            if 0 <= kh < 3 and 0 <= kw < 3:
                big[a, b, :, sy, sx, c, d, :] = weight[:, :, kh, kw].T
        return big.reshape(P, 4 * P)

    def tap1(s, a, c):
        return 2 * s + a - c

    def tap0(s, a, c):
        return 2 + c - 2 * s - a

    centre = np.zeros((C, C, 3, 3), np.float32)
    centre[np.arange(C), np.arange(C), 1, 1] = 1.0
    channel = np.arange(P) % C
    same_group = (channel[:, None] // 2 == channel[None, :] // 2).astype(np.float32)
    arrays = {
        "x": np.ascontiguousarray(cells).reshape(B, P, CELLS),
        "w0": toeplitz(L0_conv_weight, tap0),
        "w1": toeplitz(L1_conv_weight, tap1),
        "ident": toeplitz(centre, tap1),
        "g": same_group / np.float32(8),
        "bias0": np.tile(np.asarray(L0_conv_bias), 4).reshape(P, 1),
        "bias1": np.tile(np.asarray(L1_conv_bias), 4).reshape(P, 1),
    }
    nc = bacc.Bacc("TRN2", target_bir_lowering=False, num_devices=1)
    args = [nc.dram_tensor(name, a.shape, F32, kind="ExternalInput").ap() for name, a in arrays.items()]
    out = nc.dram_tensor("out", (B, P, VALID), F32, kind="ExternalOutput").ap()
    conv_blocks(nc, *args, out)
    r = run_bass_kernel_spmd(nc, [arrays], core_ids=[0])
    got = r.results[0]["out"].reshape(B, 2, 2, C, OUT, OUT)
    return got.transpose(0, 3, 4, 1, 5, 2).reshape(B, C, H, W)
```
